# Optimizing a Trainium2 kernel written in Bass

```python
import numpy as np
import jax
import jax.numpy as jnp

def _softmax(x, axis=-1):
    return jax.nn.softmax(x, axis=axis)
def _gelu(x):
    return jax.nn.gelu(x, approximate=True)
def _silu(x):
    return jax.nn.silu(x)
def _sigmoid(x):
    return jax.nn.sigmoid(x)
def _layernorm(x, axis=-1, eps=1e-5):
    m = jnp.mean(x, axis=axis, keepdims=True)
    v = jnp.var(x, axis=axis, keepdims=True)
    return (x - m) / jnp.sqrt(v + eps)
def _scatter_add(tgt, idx, src, axis=0):
    return tgt.at[idx].add(src)
def _segment_sum(src, seg, n):
    return jax.ops.segment_sum(src, seg, n)

kernel_name = 'mk_rec_standalone_d1_rec_44c253'

def setup_inputs(seed: int = 0):
    np.random.seed(seed)
    _w = jnp.asarray
    def _rec_inputs():
        import jax
        import jax.numpy as jnp
        _rk = jax.random.key(seed)
        r_x = jax.random.randint(jax.random.fold_in(_rk, 1), (1024, 50000), 0, 2, jnp.int32)
        return r_x
    r_x = _rec_inputs()
    def _L0_rec_setup():
        import jax, jax.numpy as jnp
        import numpy as np
        B, VOCAB, F = (4096, 50000, 64)
        key = jax.random.key(seed)
        k1, k2 = jax.random.split(key, 2)
        x = jax.random.randint(k1, (B, VOCAB), 0, 2, dtype=jnp.int32)
        V = jax.random.normal(k2, (VOCAB, F), dtype=jnp.float32) * 0.05
        bias = jnp.zeros((VOCAB, 1), dtype=jnp.float32)
        g_bias = jnp.zeros((), dtype=jnp.float32)
        return {'x': x, 'V': V, 'bias': bias, 'g_bias': g_bias}
    _L0_rec_all = _L0_rec_setup()
    _L0_rec_in = {k: v for k, v in _L0_rec_all.items() if k in ('V', 'bias', 'g_bias', )}
    del _L0_rec_all

    return {
        "r_x": r_x,
        "L0_rec_V": _L0_rec_in["V"],
        "L0_rec_bias": _L0_rec_in["bias"],
        "L0_rec_g_bias": _L0_rec_in["g_bias"],
    }

def reference(r_x, L0_rec_V, L0_rec_bias, L0_rec_g_bias):
    import jax
    import jax.numpy as jnp
    def _L0_rec_ref(x, V, bias, g_bias):
        import jax, jax.numpy as jnp
        import numpy as np
        B, VOCAB, F = (4096, 50000, 64)
        xf = x.astype(V.dtype)
        xv = xf @ V
        sum_sq = jnp.sum(xv * xv, axis=-1)
        sq_sum = xf @ jnp.sum(V * V, axis=-1)
        second_order = 0.5 * (sum_sq - sq_sum)
        linear = g_bias + xf @ bias
        return linear + second_order[:, None]

    y = _L0_rec_ref(r_x, L0_rec_V, L0_rec_bias, L0_rec_g_bias)
    return y


_drawn_inputs = setup_inputs


def setup_inputs(seed=0):
    import zlib

    import numpy as np

    out = dict(_drawn_inputs(seed))
    spreads = {'L0_rec_bias': (0.0, 0.1)}
    factors = {}
    for name, (base, spread) in spreads.items():
        noise = np.random.default_rng([zlib.crc32(name.encode()), seed]).standard_normal(out[name].shape)
        drawn = base * np.exp(spread * noise) if base else spread * noise
        out[name] = jnp.asarray(drawn.astype(out[name].dtype))
    for name, factor in factors.items():
        out[name] = (out[name] * factor).astype(out[name].dtype)
    return out
```

```python
from contextlib import ExitStack

import concourse.bass as bass
from concourse import mybir

ALU = mybir.AluOpType
F32 = mybir.dt.float32
BF16 = mybir.dt.bfloat16
I32 = mybir.dt.int32
U16 = mybir.dt.uint16
AX_X = mybir.AxisListType.X

P = 128
BATCH = 1024
VOCAB = 50000
F = 64
VB = F + 1
BANK = 512
HALVES = BATCH // BANK

GROUP = 8
CHUNK = 4
PER_GROUP = GROUP // CHUNK
BODY_GROUPS = 2
BODY_CHUNKS = BODY_GROUPS * PER_GROUP
TILES = -(-VOCAB // P)
BODIES = TILES // (GROUP * BODY_GROUPS)
GROUPS = BODIES * BODY_GROUPS
CHUNKS = GROUPS * PER_GROUP
TAIL = TILES - GROUPS * GROUP
TAIL_CHUNKS = [(0, 4), (4, 2), (6, 1)]
assert TAIL == sum(n for _, n in TAIL_CHUNKS) and len(TAIL_CHUNKS) <= BODY_CHUNKS and TAIL <= GROUP

WCOLS = 2 * P
C_AT = 3 * F
NPARTS = 3
PREP_STEPS = 10
TAIL_ROW = GROUPS * GROUP * P

BF16_256 = 0x4380


def fm_kernel(nc, x_t, v_bias, g_bias, out):
    x_main = x_t[0:TAIL_ROW, :].rearrange("(g p j) b -> g p (j b)", p=P, j=GROUP)
    x_tail = x_t[TAIL_ROW:TILES * P, :].rearrange("(p j) b -> p (j b)", p=P)
    v_main = v_bias[0:TAIL_ROW, :].rearrange("(g p j) f -> g p (j f)", p=P, j=GROUP)
    v_tail = v_bias[TAIL_ROW:TILES * P, :].rearrange("(p j) f -> p (j f)", p=P)

    with ExitStack() as ctx:
        def sb(name, shape, dt):
            return ctx.enter_context(nc.sbuf_tensor(name, shape, dt))

        def sem(name):
            return ctx.enter_context(nc.semaphore(name))

        x_int = [sb(f"x_int{s}", [P, CHUNK * BATCH], I32) for s in range(BODY_CHUNKS)]
        x_bf = [sb(f"x_bf{s}", [P, CHUNK * BATCH], BF16) for s in range(BODY_CHUNKS)]
        v_raw = [sb(f"v_raw{s}", [P, GROUP * VB], F32) for s in range(BODY_GROUPS)]
        w_bf = [sb(f"w_bf{s}", [P, GROUP, WCOLS], BF16) for s in range(BODY_GROUPS)]
        v_sq = sb("v_sq", [P, GROUP, F], F32)
        v_rest = sb("v_rest", [P, GROUP, F], F32)
        v_sum = sb("v_sum", [P, GROUP], F32)
        c_full = sb("c_full", [P, GROUP], F32)
        c_rest = sb("c_rest", [P, GROUP], F32)
        top_bits = sb("top_bits", [P, CHUNK * BATCH], U16)
        top_of_row = sb("top_of_row", [P, 1], F32)
        row_wide = sb("row_wide", [P, 1], BF16)
        ones = sb("ones", [P, 1], BF16)
        wide_count = sb("wide_count", [1, 1], I32)
        mid_sb = sb("mid_sb", [F, BATCH], F32)
        low_sb = sb("low_sb", [F, BATCH], F32)
        xv = sb("xv", [F, BATCH], F32)
        terms = sb("terms", [F + NPARTS, BATCH], F32)
        term_weights = sb("term_weights", [F + NPARTS, 1], F32)
        g_sb = sb("g_sb", [1, 1], F32)
        y_sb = sb("y_sb", [1, BATCH], F32)

        acc_hm = [ctx.enter_context(nc.psum_tensor(f"acc_hm{h}", [P, BANK], F32)) for h in range(HALVES)]
        acc_lc = [ctx.enter_context(nc.psum_tensor(f"acc_lc{h}", [P, BANK], F32)) for h in range(HALVES)]
        y_ps = [ctx.enter_context(nc.psum_tensor(f"y_ps{h}", [P, BANK], F32)) for h in range(HALVES)]
        count_ps = ctx.enter_context(nc.psum_tensor("count_ps", [P, BANK], F32))

        x_landed = [sem(f"x_landed{s}") for s in range(BODY_CHUNKS)]
        v_landed = [sem(f"v_landed{s}") for s in range(BODY_GROUPS)]
        g_landed = sem("g_landed")
        constants_set = sem("constants_set")
        x_converted = sem("x_converted")
        x_checked = sem("x_checked")
        prep_step = sem("prep_step")
        w_ready = sem("w_ready")
        chunk_summed = sem("chunk_summed")
        mid_copied = sem("mid_copied")
        final_step = sem("final_step")
        terms_ready = sem("terms_ready")
        y_summed = sem("y_summed")
        y_ready = sem("y_ready")
        y_stored = sem("y_stored")
        rows_flagged = sem("rows_flagged")
        wide_counted = sem("wide_counted")
        flag_ready = sem("flag_ready")

        wx_landed = [sem(f"wx_landed{s}") for s in range(BODY_CHUNKS)]
        wv_landed = [sem(f"wv_landed{s}") for s in range(BODY_GROUPS)]
        wx_converted = sem("wx_converted")
        wv_step = sem("wv_step")
        wv_ready = sem("wv_ready")
        w_chunk_summed = sem("w_chunk_summed")
        w_terms_step = sem("w_terms_step")
        w_terms_ready = sem("w_terms_ready")
        w_y_summed = sem("w_y_summed")
        w_y_ready = sem("w_y_ready")
        w_y_stored = sem("w_y_stored")

        def half(t, h):
            return t[:, h * BANK:(h + 1) * BANK]

        block = ctx.enter_context(nc.Block())

        @block.sync
        def _(sp):
            def load_x(slot_landed, body, k):
                g = body * BODY_GROUPS + k // PER_GROUP
                at = k % PER_GROUP * CHUNK * BATCH
                sp.dma_start(x_int[k][:, :], x_main[g, :, at:at + CHUNK * BATCH]).then_inc(slot_landed[k], 16)

            def load_v(slot_landed, body, s):
                sp.dma_start(v_raw[s][:, :], v_main[body * BODY_GROUPS + s, :, :]).then_inc(slot_landed[s], 16)

            def load_body(body, first):
                for k in range(BODY_CHUNKS):
                    if k % PER_GROUP == 0:
                        s = k // PER_GROUP
                        if not first:
                            sp.wait_ge(w_ready, (body - 1) * BODY_GROUPS + s + 1)
                        load_v(v_landed, body, s)
                    if not first:
                        sp.wait_ge(x_converted, (body - 1) * BODY_CHUNKS + k + 1)
                    load_x(x_landed, body, k)

            sp.dma_start(g_sb[:, :], g_bias[:, :]).then_inc(g_landed, 16)
            load_body(0, True)
            with sp.Fori(1, BODIES) as body:
                load_body(body, False)
            sp.wait_ge(w_ready, GROUPS - BODY_GROUPS + 1)
            sp.dma_start(v_raw[0][:, 0:TAIL * VB], v_tail[:, :]).then_inc(v_landed[0], 16)
            for k, (t, n) in enumerate(TAIL_CHUNKS):
                sp.wait_ge(x_converted, CHUNKS - BODY_CHUNKS + k + 1)
                sp.dma_start(x_int[k][:, 0:n * BATCH], x_tail[:, t * BATCH:(t + n) * BATCH]).then_inc(x_landed[k], 16)

            sp.wait_ge(y_ready, HALVES)
            sp.dma_start(out[:, :], y_sb[:, :]).then_inc(y_stored, 16)
            sp.wait_ge(y_stored, 16)
            sp.wait_ge(flag_ready, 1)
            wide = sp.value_load(wide_count[0:1, 0:1], min_val=0, max_val=P)
            with sp.If(wide > 0):
                def load_wide_body(body, first):
                    for k in range(BODY_CHUNKS):
                        s, new_group = k // PER_GROUP, k % PER_GROUP == 0
                        if not first:
                            sp.wait_ge(w_chunk_summed, (body - 1) * BODY_CHUNKS + k + (PER_GROUP if new_group else 1))
                        if new_group:
                            load_v(wv_landed, body, s)
                        load_x(wx_landed, body, k)

                load_wide_body(0, True)
                with sp.Fori(1, BODIES) as body:
                    load_wide_body(body, False)
                sp.wait_ge(w_chunk_summed, CHUNKS)
                sp.dma_start(v_raw[0][:, 0:TAIL * VB], v_tail[:, :]).then_inc(wv_landed[0], 16)
                for k, (t, n) in enumerate(TAIL_CHUNKS):
                    sp.dma_start(x_int[k][:, 0:n * BATCH],
                                 x_tail[:, t * BATCH:(t + n) * BATCH]).then_inc(wx_landed[k], 16)
                sp.wait_ge(w_y_ready, HALVES)
                sp.dma_start(out[:, :], y_sb[:, :]).then_inc(w_y_stored, 16)
                sp.wait_ge(w_y_stored, 16)

        @block.scalar
        def _(act):
            def convert(body, k, first, n=CHUNK):
                done = body * BODY_CHUNKS + k
                act.wait_ge(x_landed[k], (body + 1) * 16)
                if not first:
                    act.wait_ge(chunk_summed, done - BODY_CHUNKS + 1)
                    act.wait_ge(x_checked, done - BODY_CHUNKS + 1)
                nc.scalar.copy(x_bf[k][:, 0:n * BATCH], x_int[k][:, 0:n * BATCH]).then_inc(x_converted, 1)

            for k in range(BODY_CHUNKS):
                convert(0, k, True)
            with act.Fori(1, BODIES) as body:
                for k in range(BODY_CHUNKS):
                    convert(body, k, False)
            for k, (_, n) in enumerate(TAIL_CHUNKS):
                convert(BODIES, k, False, n)
            act.wait_ge(chunk_summed, CHUNKS + len(TAIL_CHUNKS))
            for h in range(HALVES):
                nc.scalar.copy(half(mid_sb, h), acc_hm[h][F:2 * F, :]).then_inc(mid_copied, 1)

            act.wait_ge(flag_ready, 1)
            wide = act.value_load(wide_count[0:1, 0:1], min_val=0, max_val=P)
            with act.If(wide > 0):
                def convert_wide(body, k, n=CHUNK):
                    act.wait_ge(wx_landed[k], (body + 1) * 16)
                    x = x_int[k][:, 0:n * BATCH]
                    nc.scalar.copy(x.bitcast(F32), x).then_inc(wx_converted, 1)

                with act.Fori(0, BODIES) as body:
                    for k in range(BODY_CHUNKS):
                        convert_wide(body, k)
                for k, (_, n) in enumerate(TAIL_CHUNKS):
                    convert_wide(BODIES, k, n)

        @block.vector
        def _(dve):
            def split_group(g, s, first, n=GROUP):
                v = v_raw[s][:, 0:n * VB].rearrange("p (j f) -> p j f", f=VB)
                w, base = w_bf[s], g * PREP_STEPS
                hi, mid, lo = (w[:, 0:n, q * F:(q + 1) * F] for q in range(NPARTS))
                c_hi, c_mid, c_lo = (w[:, 0:n, C_AT + q] for q in range(NPARTS))
                sq, rest = v_sq[:, 0:n, :], v_rest[:, 0:n, :]
                dve.wait_ge(v_landed[s], (g // BODY_GROUPS + 1) * 16 if isinstance(g, int) else first)
                if not isinstance(g, int) or g >= BODY_GROUPS:
                    dve.wait_ge(chunk_summed, (g - BODY_GROUPS + 1) * PER_GROUP)
                nc.vector.tensor_copy(hi, v[:, :, 0:F]).then_inc(prep_step, 1)
                nc.vector.tensor_tensor(sq, v[:, :, 0:F], v[:, :, 0:F], ALU.mult).then_inc(prep_step, 1)
                dve.wait_ge(prep_step, base + 1)
                nc.vector.tensor_tensor(rest, v[:, :, 0:F], hi, ALU.subtract).then_inc(prep_step, 1)
                dve.wait_ge(prep_step, base + 2)
                nc.vector.reduce_sum(v_sum[:, 0:n], sq, AX_X).then_inc(prep_step, 1)
                dve.wait_ge(prep_step, base + 3)
                nc.vector.tensor_copy(mid, rest).then_inc(prep_step, 1)
                dve.wait_ge(prep_step, base + 4)
                nc.vector.scalar_tensor_tensor(c_full[:, 0:n], v_sum[:, 0:n], -0.5, v[:, :, F],
                                               ALU.mult, ALU.add).then_inc(prep_step, 1)
                dve.wait_ge(prep_step, base + 5)
                nc.vector.tensor_tensor(lo, rest, mid, ALU.subtract).then_inc(prep_step, 1)
                dve.wait_ge(prep_step, base + 6)
                nc.vector.tensor_copy(c_hi, c_full[:, 0:n]).then_inc(prep_step, 1)
                dve.wait_ge(prep_step, base + 8)
                nc.vector.tensor_tensor(c_rest[:, 0:n], c_full[:, 0:n], c_hi, ALU.subtract).then_inc(prep_step, 1)
                dve.wait_ge(prep_step, base + 9)
                nc.vector.tensor_copy(c_mid, c_rest[:, 0:n]).then_inc(prep_step, 1)
                dve.wait_ge(prep_step, base + 10)
                nc.vector.tensor_tensor(c_lo, c_rest[:, 0:n], c_mid, ALU.subtract).then_inc(w_ready, 1)

            def check(c, k, n=CHUNK):
                dve.wait_ge(x_converted, c + 1)
                dve.wait_ge(x_checked, c)
                top = top_bits[:, 0:n * BATCH]
                nc.vector.tensor_tensor(top, top, x_bf[k][:, 0:n * BATCH].bitcast(U16), ALU.max).then_inc(x_checked, 1)

            def body_steps(body, tail_next):
                for s in range(BODY_GROUPS):
                    g = body * BODY_GROUPS + s + 1
                    nxt = (s + 1) % BODY_GROUPS
                    landed = (body + 1 + (s + 1) // BODY_GROUPS) * 16
                    for q in range(PER_GROUP):
                        k = s * PER_GROUP + q
                        check(body * BODY_CHUNKS + k, k)
                        if q == 0:
                            split_group(g, nxt, landed, TAIL if tail_next and s == BODY_GROUPS - 1 else GROUP)

            for s in range(BODY_GROUPS):
                nc.vector.memset(w_bf[s][:, :, :], 0.0).then_inc(constants_set, 1)
            nc.vector.memset(top_bits[:, :], 0).then_inc(constants_set, 1)
            nc.vector.memset(ones[:, :], 1.0).then_inc(constants_set, 1)
            nc.vector.memset(term_weights[0:F, :], 0.5).then_inc(constants_set, 1)
            nc.vector.memset(term_weights[F:F + NPARTS, :], 1.0).then_inc(constants_set, 1)
            dve.wait_ge(constants_set, BODY_GROUPS + 4)
            split_group(0, 0, 16)
            body_steps(0, False)
            with dve.Fori(1, BODIES - 1) as body:
                body_steps(body, False)
            body_steps(BODIES - 1, True)
            for k, (_, n) in enumerate(TAIL_CHUNKS):
                check(CHUNKS + k, k, n)

            dve.wait_ge(x_checked, CHUNKS + len(TAIL_CHUNKS))
            nc.vector.tensor_reduce(top_of_row[:, :], top_bits[:, :], AX_X, ALU.max).then_inc(final_step, 1)
            dve.wait_ge(final_step, 1)
            nc.vector.tensor_scalar(row_wide[:, :], top_of_row[:, :], float(BF16_256), None,
                                    ALU.is_ge).then_inc(rows_flagged, 1)

            for h in range(HALVES):
                dve.wait_ge(chunk_summed, CHUNKS + len(TAIL_CHUNKS))
                nc.vector.tensor_copy(half(terms, h)[F:F + NPARTS, :],
                                      acc_lc[h][F:F + NPARTS, :]).then_inc(final_step, 1)
                dve.wait_ge(mid_copied, h + 1)
                nc.vector.tensor_tensor(half(low_sb, h), acc_lc[h][0:F, :], half(mid_sb, h),
                                        ALU.add).then_inc(final_step, 1)
                dve.wait_ge(final_step, 4 * h + 3)
                nc.vector.tensor_tensor(half(xv, h), acc_hm[h][0:F, :], half(low_sb, h), ALU.add).then_inc(final_step, 1)
                dve.wait_ge(final_step, 4 * h + 4)
                nc.vector.tensor_tensor(half(terms, h)[0:F, :], half(xv, h), half(xv, h),
                                        ALU.mult).then_inc(final_step, 1)
            dve.wait_ge(wide_counted, 1)
            nc.vector.tensor_copy(wide_count[:, :], count_ps[0:1, 0:1]).then_inc(flag_ready, 1)
            dve.wait_ge(g_landed, 16)
            for h in range(HALVES):
                dve.wait_ge(y_summed, h + 1)
                nc.vector.tensor_scalar(half(y_sb, h), y_ps[h][0:1, :], g_sb[:, :], None, ALU.add).then_inc(y_ready, 1)

            dve.wait_ge(flag_ready, 1)
            wide = dve.value_load(wide_count[0:1, 0:1], min_val=0, max_val=P)
            with dve.If(wide > 0):
                def prepare_wide(g, s, landed, n=GROUP):
                    v = v_raw[s][:, 0:n * VB].rearrange("p (j f) -> p j f", f=VB)
                    dve.wait_ge(wv_landed[s], landed)
                    nc.vector.tensor_tensor(v_sq[:, 0:n, :], v[:, :, 0:F], v[:, :, 0:F], ALU.mult).then_inc(wv_step, 1)
                    dve.wait_ge(wv_step, 2 * g + 1)
                    nc.vector.reduce_sum(v_sum[:, 0:n], v_sq[:, 0:n, :], AX_X).then_inc(wv_step, 1)
                    dve.wait_ge(wv_step, 2 * g + 2)
                    nc.vector.scalar_tensor_tensor(v[:, :, F], v_sum[:, 0:n], -0.5, v[:, :, F],
                                                   ALU.mult, ALU.add).then_inc(wv_ready, 1)

                with dve.Fori(0, BODIES) as body:
                    for s in range(BODY_GROUPS):
                        prepare_wide(body * BODY_GROUPS + s, s, (body + 1) * 16)
                prepare_wide(GROUPS, 0, (BODIES + 1) * 16, TAIL)
                dve.wait_ge(w_chunk_summed, CHUNKS + len(TAIL_CHUNKS))
                for h in range(HALVES):
                    nc.vector.tensor_copy(half(terms, h)[F:VB, :], acc_hm[h][F:VB, :]).then_inc(w_terms_step, 1)
                    nc.vector.tensor_copy(half(xv, h), acc_hm[h][0:F, :]).then_inc(w_terms_step, 1)
                    dve.wait_ge(w_terms_step, 2 * h + 2)
                    nc.vector.tensor_tensor(half(terms, h)[0:F, :], half(xv, h), half(xv, h),
                                            ALU.mult).then_inc(w_terms_ready, 1)
                dve.wait_ge(y_stored, 16)
                for h in range(HALVES):
                    dve.wait_ge(w_y_summed, h + 1)
                    nc.vector.tensor_scalar(half(y_sb, h), y_ps[h][0:1, :], g_sb[:, :], None,
                                            ALU.add).then_inc(w_y_ready, 1)

        @block.tensor
        def _(pe):
            def multiply(c, k, s, j0, first, last, n=CHUNK):
                pe.wait_ge(x_converted, c + 1)
                for j in range(n):
                    w = w_bf[s][:, j0 + j, :]
                    start, stop = first and j == 0, last and j == n - 1
                    for acc, cols in ((acc_hm, w[:, 0:P]), (acc_lc, w[:, P:WCOLS])):
                        for h in range(HALVES):
                            at = j * BATCH + h * BANK
                            mm = nc.tensor.matmul(acc[h][:, :], cols, x_bf[k][:, at:at + BANK], start=start, stop=stop)
                mm.then_inc(chunk_summed, 1)

            def body_products(body, first):
                for k in range(BODY_CHUNKS):
                    s = k // PER_GROUP
                    if k % PER_GROUP == 0:
                        pe.wait_ge(w_ready, body * BODY_GROUPS + s + 1)
                    multiply(body * BODY_CHUNKS + k, k, s, k % PER_GROUP * CHUNK, first and k == 0, False)

            body_products(0, True)
            with pe.Fori(1, BODIES) as body:
                body_products(body, False)
            pe.wait_ge(w_ready, GROUPS + 1)
            for k, (t, n) in enumerate(TAIL_CHUNKS):
                multiply(CHUNKS + k, k, 0, t, False, k == len(TAIL_CHUNKS) - 1, n)

            pe.wait_ge(constants_set, BODY_GROUPS + 4)
            pe.wait_ge(rows_flagged, 1)
            nc.tensor.matmul(count_ps[0:1, 0:1], row_wide[:, :], ones[:, :], start=True, stop=True).then_inc(wide_counted, 1)
            for h in range(HALVES):
                pe.wait_ge(final_step, 4 * h + 5)
                nc.tensor.matmul(y_ps[h][0:1, :], term_weights[:, :], half(terms, h), start=True, stop=True).then_inc(y_summed, 1)

            pe.wait_ge(flag_ready, 1)
            wide = pe.value_load(wide_count[0:1, 0:1], min_val=0, max_val=P)
            with pe.If(wide > 0):
                def multiply_wide(c, k, s, j0, first, last, n=CHUNK):
                    pe.wait_ge(wx_converted, c + 1)
                    for j in range(n):
                        w = v_raw[s][:, (j0 + j) * VB:(j0 + j + 1) * VB]
                        start, stop = first and j == 0, last and j == n - 1
                        for h in range(HALVES):
                            at = j * BATCH + h * BANK
                            mm = nc.tensor.matmul(acc_hm[h][0:VB, :], w, x_int[k][:, at:at + BANK].bitcast(F32),
                                                  start=start, stop=stop)
                    mm.then_inc(w_chunk_summed, 1)

                def wide_products(body, first):
                    for k in range(BODY_CHUNKS):
                        s = k // PER_GROUP
                        if k % PER_GROUP == 0:
                            pe.wait_ge(wv_ready, body * BODY_GROUPS + s + 1)
                        multiply_wide(body * BODY_CHUNKS + k, k, s, k % PER_GROUP * CHUNK, first and k == 0, False)

                wide_products(0, True)
                with pe.Fori(1, BODIES) as body:
                    wide_products(body, False)
                pe.wait_ge(wv_ready, GROUPS + 1)
                for k, (t, n) in enumerate(TAIL_CHUNKS):
                    multiply_wide(CHUNKS + k, k, 0, t, False, k == len(TAIL_CHUNKS) - 1, n)
                for h in range(HALVES):
                    pe.wait_ge(w_terms_ready, h + 1)
                    nc.tensor.matmul(y_ps[h][0:1, :], term_weights[0:VB, :], terms[0:VB, h * BANK:(h + 1) * BANK],
                                     start=True, stop=True).then_inc(w_y_summed, 1)


def kernel(r_x, L0_rec_V, L0_rec_bias, L0_rec_g_bias):
    import numpy as _np
    import concourse.bacc as _bacc
    from concourse import mybir as _mybir
    from concourse.bass_utils import run_bass_kernel_spmd as _run

    rows = TILES * P
    x_t = _np.zeros((rows, BATCH), _np.int32)
    x_t[:VOCAB] = _np.asarray(r_x).T
    v_bias = _np.zeros((rows, VB), _np.float32)
    v_bias[:VOCAB, :F] = _np.asarray(L0_rec_V)
    v_bias[:VOCAB, F:] = _np.asarray(L0_rec_bias)
    arrays = {"x_t": x_t, "v_bias": v_bias, "g_bias": _np.asarray(L0_rec_g_bias).reshape(1, 1)}

    nc = _bacc.Bacc("TRN2", target_bir_lowering=False, num_devices=1)
    args = [nc.dram_tensor(n, a.shape, _mybir.dt.from_np(a.dtype), kind="ExternalInput").ap() for n, a in arrays.items()]
    args.append(nc.dram_tensor("out", (1, BATCH), _mybir.dt.float32, kind="ExternalOutput").ap())
    fm_kernel(nc, *args)
    r = _run(nc, [arrays], core_ids=[0])
    return r.results[0]["out"].reshape(BATCH, 1)
```

```python
from contextlib import ExitStack

import concourse.bass as bass
from concourse import mybir

ALU = mybir.AluOpType
ACT = mybir.ActivationFunctionType
F32 = mybir.dt.float32
BF16 = mybir.dt.bfloat16
I32 = mybir.dt.int32
U16 = mybir.dt.uint16
AX_X = mybir.AxisListType.X

P = 128
BATCH = 1024
VOCAB = 50000
F = 64
VB = F + 1
BANK = 512
HALVES = BATCH // BANK
COLS = BATCH // P

GROUP = 8
CHUNK = 2
PER_GROUP = GROUP // CHUNK
BODY_GROUPS = 2
BODY_CHUNKS = BODY_GROUPS * PER_GROUP
TILES = -(-VOCAB // P)
BODIES = TILES // (GROUP * BODY_GROUPS)
GROUPS = BODIES * BODY_GROUPS
CHUNKS = GROUPS * PER_GROUP
TAIL = TILES - GROUPS * GROUP
TAIL_ROW = GROUPS * GROUP * P
LAST_ROWS = VOCAB - (TILES - 1) * P

FULL = TAIL - 1
PAIRS = [(t, min(2, FULL - t), P) for t in range(0, FULL, 2)]
TAIL_CHUNKS = [(h, *piece) for h in range(HALVES) for piece in (*PAIRS, (FULL, 1, LAST_ROWS))]
ALL_CHUNKS = CHUNKS + len(TAIL_CHUNKS)
FIRST_HALF_CHUNKS = ALL_CHUNKS - len(TAIL_CHUNKS) // HALVES
HALF_0_AFTER = FIRST_HALF_CHUNKS
HALF_CHUNKS = [FIRST_HALF_CHUNKS, ALL_CHUNKS]
assert HALVES == 2 and 1 < TAIL <= GROUP and CHUNK * BATCH >= 2 * BANK

WCOLS = 2 * P
C_AT = 3 * F
NPARTS = 3
PREP_STEPS = 10

BF16_256 = 0x4380


def fm_kernel(nc, x_t, v_main, v_tail, g_bias, out):
    x_main = x_t[0:TAIL_ROW, :].rearrange("(c p j) b -> c p (j b)", p=P, j=CHUNK)
    x_full = x_t[TAIL_ROW:TAIL_ROW + FULL * P, :].rearrange("(t p) b -> p t b", p=P)
    x_last = x_t[TAIL_ROW + FULL * P:VOCAB, :]

    with ExitStack() as ctx:
        def sb(name, shape, dt):
            return ctx.enter_context(nc.sbuf_tensor(name, shape, dt))

        def sem(name):
            return ctx.enter_context(nc.semaphore(name))

        x_int = [sb(f"x_int{s}", [P, CHUNK * BATCH], I32) for s in range(BODY_CHUNKS)]
        x_bf = [sb(f"x_bf{s}", [P, CHUNK * BATCH], BF16) for s in range(BODY_CHUNKS)]
        v_raw = [sb(f"v_raw{s}", [P, GROUP * VB], F32) for s in range(BODY_GROUPS)]
        w_bf = [sb(f"w_bf{s}", [P, GROUP, WCOLS], BF16) for s in range(BODY_GROUPS)]
        v_raw_tail = sb("v_raw_tail", [P, TAIL * VB], F32)
        w_bf_tail = sb("w_bf_tail", [P, TAIL, WCOLS], BF16)
        v_sq = sb("v_sq", [P, GROUP, F], F32)
        v_rest = sb("v_rest", [P, GROUP, F], F32)
        v_sum = sb("v_sum", [P, GROUP], F32)
        c_full = sb("c_full", [P, GROUP], F32)
        c_rest = sb("c_rest", [P, GROUP], F32)
        top_bits = sb("top_bits", [P, CHUNK * BATCH], U16)
        top_of_row = sb("top_of_row", [P, 1], F32)
        row_wide = sb("row_wide", [P, 1], BF16)
        ones = sb("ones", [P, 1], BF16)
        wide_count = sb("wide_count", [1, 1], I32)
        mid_sb = sb("mid_sb", [F, BATCH], F32)
        low_sb = sb("low_sb", [F, BATCH], F32)
        xv = sb("xv", [F, BATCH], F32)
        terms = sb("terms", [F + NPARTS, BATCH], F32)
        term_weights = sb("term_weights", [F + NPARTS, 1], F32)
        g_sb = sb("g_sb", [P, 1], F32)
        y_sb = sb("y_sb", [P, COLS], F32)

        acc_hm = [ctx.enter_context(nc.psum_tensor(f"acc_hm{h}", [P, BANK], F32)) for h in range(HALVES)]
        acc_lc = [ctx.enter_context(nc.psum_tensor(f"acc_lc{h}", [P, BANK], F32)) for h in range(HALVES)]
        y_ps = ctx.enter_context(nc.psum_tensor("y_ps", [P, BANK], F32))
        count_ps = ctx.enter_context(nc.psum_tensor("count_ps", [P, BANK], F32))

        x_landed = [sem(f"x_landed{s}") for s in range(BODY_CHUNKS)]
        v_landed = [sem(f"v_landed{s}") for s in range(BODY_GROUPS)]
        v_tail_landed = sem("v_tail_landed")
        g_landed = sem("g_landed")
        constants_set = sem("constants_set")
        x_converted = sem("x_converted")
        x_checked = sem("x_checked")
        prep_step = sem("prep_step")
        w_ready = sem("w_ready")
        tail_prep_step = sem("tail_prep_step")
        w_tail_ready = sem("w_tail_ready")
        chunk_summed = sem("chunk_summed")
        top_folded = sem("top_folded")
        mid_copied = sem("mid_copied")
        low_added = sem("low_added")
        xv_ready = sem("xv_ready")
        squares_ready = sem("squares_ready")
        c_copied = sem("c_copied")
        y_summed = sem("y_summed")
        y_ready = sem("y_ready")
        y_stored = sem("y_stored")
        rows_flagged = sem("rows_flagged")
        wide_counted = sem("wide_counted")
        flag_ready = sem("flag_ready")

        wide_x_landed = [sem(f"wide_x_landed{s}") for s in range(BODY_CHUNKS)]
        wide_v_landed = [sem(f"wide_v_landed{s}") for s in range(BODY_GROUPS)]
        wide_x_converted = sem("wide_x_converted")
        wide_v_step = sem("wide_v_step")
        wide_v_ready = sem("wide_v_ready")
        wide_v_tail_ready = sem("wide_v_tail_ready")
        wide_chunk_summed = sem("wide_chunk_summed")
        wide_terms_step = sem("wide_terms_step")
        wide_squares_ready = sem("wide_squares_ready")
        wide_y_summed = sem("wide_y_summed")
        wide_y_ready = sem("wide_y_ready")
        wide_y_stored = sem("wide_y_stored")

        def half(t, h):
            return t[:, h * BANK:(h + 1) * BANK]

        block = ctx.enter_context(nc.Block())

        @block.sync
        def _(sp):
            def load_x(slot_landed, body, k):
                sp.dma_start(x_int[k][:, :], x_main[body * BODY_CHUNKS + k, :, :]).then_inc(slot_landed[k], 16)

            def load_v(slot_landed, body, s):
                sp.dma_start(v_raw[s][:, :], v_main[body * BODY_GROUPS + s, :, :]).then_inc(slot_landed[s], 16)

            def load_body(body, first):
                for k in range(BODY_CHUNKS):
                    if k % PER_GROUP == 0:
                        s = k // PER_GROUP
                        if not first:
                            sp.wait_ge(w_ready, (body - 1) * BODY_GROUPS + s + 1)
                        load_v(v_landed, body, s)
                    if not first:
                        sp.wait_ge(x_converted, (body - 1) * BODY_CHUNKS + k + 1)
                    load_x(x_landed, body, k)

            def load_tail(slot_landed, c):
                h, t, n, rows = TAIL_CHUNKS[c - CHUNKS]
                slot, cols = c % BODY_CHUNKS, slice(h * BANK, (h + 1) * BANK)
                if rows == P:
                    sp.dma_start(x_int[slot][:, 0:n * BANK].rearrange("p (t b) -> p t b", b=BANK),
                                 x_full[:, t:t + n, cols]).then_inc(slot_landed[slot], 16)
                else:
                    sp.dma_start(x_int[slot][0:rows, 0:BANK], x_last[:, cols]).then_inc(slot_landed[slot], 16)

            load_body(0, True)
            sp.dma_start(v_raw_tail[:, :], v_tail[:, :]).then_inc(v_tail_landed, 16)
            sp.dma_start(g_sb[:, :], g_bias[:, :]).then_inc(g_landed, 16)
            with sp.Fori(1, BODIES) as body:
                load_body(body, False)
            for c in range(CHUNKS, ALL_CHUNKS):
                sp.wait_ge(x_converted, c - BODY_CHUNKS + 1)
                load_tail(x_landed, c)

            sp.wait_ge(y_ready, 1)
            sp.dma_start(out[:, :], y_sb[:, :]).then_inc(y_stored, 16)
            sp.wait_ge(flag_ready, 1)
            wide = sp.value_load(wide_count[0:1, 0:1], min_val=0, max_val=P)
            with sp.If(wide > 0):
                def load_wide_body(body, first):
                    for k in range(BODY_CHUNKS):
                        s, new_group = k // PER_GROUP, k % PER_GROUP == 0
                        if not first:
                            sp.wait_ge(wide_chunk_summed, (body - 1) * BODY_CHUNKS + k + (PER_GROUP if new_group else 1))
                        if new_group:
                            load_v(wide_v_landed, body, s)
                        load_x(wide_x_landed, body, k)

                load_wide_body(0, True)
                with sp.Fori(1, BODIES) as body:
                    load_wide_body(body, False)
                sp.wait_ge(wide_chunk_summed, CHUNKS)
                for c in range(CHUNKS, ALL_CHUNKS):
                    if c >= CHUNKS + BODY_CHUNKS:
                        sp.wait_ge(wide_chunk_summed, c - BODY_CHUNKS + 1)
                    load_tail(wide_x_landed, c)
                sp.wait_ge(wide_y_ready, 1)
                sp.dma_start(out[:, :], y_sb[:, :]).then_inc(wide_y_stored, 16)
                sp.wait_ge(wide_y_stored, 16)
            sp.wait_ge(y_stored, 16)

        @block.scalar
        def _(act):
            def convert(body, k, first, width=CHUNK * BATCH, rows=P):
                done = body * BODY_CHUNKS + k
                act.wait_ge(x_landed[k], (body + 1) * 16)
                if not first:
                    act.wait_ge(chunk_summed, done - BODY_CHUNKS + 1)
                    act.wait_ge(x_checked, done - BODY_CHUNKS + 1)
                nc.scalar.copy(x_bf[k][0:rows, 0:width], x_int[k][0:rows, 0:width]).then_inc(x_converted, 1)

            for k in range(BODY_CHUNKS):
                convert(0, k, True)
            with act.Fori(1, BODIES) as body:
                for k in range(BODY_CHUNKS):
                    convert(body, k, False)
            def move_mid(h):
                act.wait_ge(chunk_summed, HALF_CHUNKS[h])
                nc.scalar.copy(half(mid_sb, h), acc_hm[h][F:2 * F, :]).then_inc(mid_copied, 1)

            def move_c(h):
                nc.scalar.copy(half(terms, h)[F:F + NPARTS, :], acc_lc[h][F:F + NPARTS, :]).then_inc(c_copied, 1)

            for c in range(CHUNKS, ALL_CHUNKS):
                _, _, n, rows = TAIL_CHUNKS[c - CHUNKS]
                convert(c // BODY_CHUNKS, c % BODY_CHUNKS, False, n * BANK, rows)
                if c == HALF_0_AFTER:
                    move_mid(0)
            move_c(0)
            move_mid(1)
            move_c(1)
            act.wait_ge(g_landed, 16)
            act.wait_ge(y_summed, HALVES)
            nc.scalar.activation(y_sb[:, :], y_ps[:, 0:COLS], ACT.Identity, bias=g_sb[:, :]).then_inc(y_ready, 1)

            act.wait_ge(flag_ready, 1)
            wide = act.value_load(wide_count[0:1, 0:1], min_val=0, max_val=P)
            with act.If(wide > 0):
                def convert_wide(body, k, width=CHUNK * BATCH, rows=P):
                    act.wait_ge(wide_x_landed[k], (body + 1) * 16)
                    x = x_int[k][0:rows, 0:width]
                    nc.scalar.copy(x.bitcast(F32), x).then_inc(wide_x_converted, 1)

                with act.Fori(0, BODIES) as body:
                    for k in range(BODY_CHUNKS):
                        convert_wide(body, k)
                for c in range(CHUNKS, ALL_CHUNKS):
                    _, _, n, rows = TAIL_CHUNKS[c - CHUNKS]
                    convert_wide(c // BODY_CHUNKS, c % BODY_CHUNKS, n * BANK, rows)

        @block.vector
        def _(dve):
            def split(v, w, n, step, base, ready):
                v = v[:, :].rearrange("p (j f) -> p j f", f=VB)
                hi, mid, lo = (w[:, 0:n, q * F:(q + 1) * F] for q in range(NPARTS))
                c_hi, c_mid, c_lo = (w[:, 0:n, C_AT + q] for q in range(NPARTS))
                sq, rest = v_sq[:, 0:n, :], v_rest[:, 0:n, :]
                nc.vector.tensor_copy(hi, v[:, :, 0:F]).then_inc(step, 1)
                nc.vector.tensor_tensor(sq, v[:, :, 0:F], v[:, :, 0:F], ALU.mult).then_inc(step, 1)
                dve.wait_ge(step, base + 1)
                nc.vector.tensor_tensor(rest, v[:, :, 0:F], hi, ALU.subtract).then_inc(step, 1)
                dve.wait_ge(step, base + 2)
                nc.vector.reduce_sum(v_sum[:, 0:n], sq, AX_X).then_inc(step, 1)
                dve.wait_ge(step, base + 3)
                nc.vector.tensor_copy(mid, rest).then_inc(step, 1)
                dve.wait_ge(step, base + 4)
                nc.vector.scalar_tensor_tensor(c_full[:, 0:n], v_sum[:, 0:n], -0.5, v[:, :, F],
                                               ALU.mult, ALU.add).then_inc(step, 1)
                dve.wait_ge(step, base + 5)
                nc.vector.tensor_tensor(lo, rest, mid, ALU.subtract).then_inc(step, 1)
                dve.wait_ge(step, base + 6)
                nc.vector.tensor_copy(c_hi, c_full[:, 0:n]).then_inc(step, 1)
                dve.wait_ge(step, base + 8)
                nc.vector.tensor_tensor(c_rest[:, 0:n], c_full[:, 0:n], c_hi, ALU.subtract).then_inc(step, 1)
                dve.wait_ge(step, base + 9)
                nc.vector.tensor_copy(c_mid, c_rest[:, 0:n]).then_inc(step, 1)
                dve.wait_ge(step, base + 10)
                nc.vector.tensor_tensor(c_lo, c_rest[:, 0:n], c_mid, ALU.subtract).then_inc(ready, 1)

            def split_group(g, s, landed, reused=True):
                dve.wait_ge(v_landed[s], landed)
                if reused:
                    dve.wait_ge(chunk_summed, (g - BODY_GROUPS + 1) * PER_GROUP)
                split(v_raw[s], w_bf[s], GROUP, prep_step, g * PREP_STEPS, w_ready)

            def check(c, k, width=CHUNK * BATCH, rows=P):
                dve.wait_ge(x_converted, c + 1)
                if not isinstance(c, int) or c > 0:
                    dve.wait_ge(x_checked, c)
                top = top_bits[0:rows, 0:width]
                nc.vector.tensor_tensor(top, top, x_bf[k][0:rows, 0:width].bitcast(U16), ALU.max).then_inc(x_checked, 1)

            def body_steps(body, first=False, last=False):
                for s in range(BODY_GROUPS):
                    g = body * BODY_GROUPS + s + 1
                    nxt = (s + 1) % BODY_GROUPS
                    landed = (body + 1 + (s + 1) // BODY_GROUPS) * 16
                    for q in range(PER_GROUP):
                        k = s * PER_GROUP + q
                        check(body * BODY_CHUNKS + k, k)
                        if q == 0 and not (last and s == BODY_GROUPS - 1):
                            split_group(g, nxt, landed, not first or s + 1 >= BODY_GROUPS)

            for s in range(BODY_GROUPS):
                nc.vector.memset(w_bf[s][:, :, :], 0.0).then_inc(constants_set, 1)
            nc.vector.memset(w_bf_tail[:, :, :], 0.0).then_inc(constants_set, 1)
            nc.vector.memset(top_bits[:, :], 0).then_inc(constants_set, 1)
            nc.vector.memset(ones[:, :], 1.0).then_inc(constants_set, 1)
            nc.vector.memset(term_weights[0:F, :], 0.5).then_inc(constants_set, 1)
            nc.vector.memset(term_weights[F:F + NPARTS, :], 1.0).then_inc(constants_set, 1)
            dve.wait_ge(constants_set, BODY_GROUPS + 5)
            split_group(0, 0, 16, False)
            body_steps(0, first=True)
            dve.wait_ge(v_tail_landed, 16)
            split(v_raw_tail, w_bf_tail, TAIL, tail_prep_step, 0, w_tail_ready)
            with dve.Fori(1, BODIES - 1) as body:
                body_steps(body)
            body_steps(BODIES - 1, last=True)
            width, folds = CHUNK * BATCH, 0
            while width > 2 * BANK:
                width //= 2
                if folds:
                    dve.wait_ge(top_folded, folds)
                else:
                    dve.wait_ge(x_checked, CHUNKS)
                nc.vector.tensor_tensor(top_bits[:, 0:width], top_bits[:, 0:width], top_bits[:, width:2 * width],
                                        ALU.max).then_inc(top_folded, 1)
                folds += 1
            dve.wait_ge(top_folded, folds)

            def check_tail(c):
                _, _, n, rows = TAIL_CHUNKS[c - CHUNKS]
                check(c, c % BODY_CHUNKS, n * BANK, rows)

            def square(h):
                dve.wait_ge(chunk_summed, HALF_CHUNKS[h])
                dve.wait_ge(mid_copied, h + 1)
                nc.vector.tensor_tensor(half(low_sb, h), acc_lc[h][0:F, :], half(mid_sb, h), ALU.add).then_inc(low_added, 1)
                dve.wait_ge(low_added, h + 1)
                nc.vector.tensor_tensor(half(xv, h), acc_hm[h][0:F, :], half(low_sb, h), ALU.add).then_inc(xv_ready, 1)
                dve.wait_ge(xv_ready, h + 1)
                nc.vector.tensor_tensor(half(terms, h)[0:F, :], half(xv, h), half(xv, h),
                                        ALU.mult).then_inc(squares_ready, 1)

            for c in range(CHUNKS, ALL_CHUNKS - 1):
                check_tail(c)
                if c == HALF_0_AFTER:
                    square(0)
            square(1)
            check_tail(ALL_CHUNKS - 1)
            dve.wait_ge(x_checked, ALL_CHUNKS)
            nc.vector.tensor_reduce(top_of_row[:, :], top_bits[:, 0:2 * BANK], AX_X, ALU.max).then_inc(top_folded, 1)
            dve.wait_ge(top_folded, folds + 1)
            nc.vector.tensor_scalar(row_wide[:, :], top_of_row[:, :], float(BF16_256), None,
                                    ALU.is_ge).then_inc(rows_flagged, 1)
            dve.wait_ge(wide_counted, 1)
            nc.vector.tensor_copy(wide_count[:, :], count_ps[0:1, 0:1]).then_inc(flag_ready, 1)

            dve.wait_ge(flag_ready, 1)
            wide = dve.value_load(wide_count[0:1, 0:1], min_val=0, max_val=P)
            with dve.If(wide > 0):
                def prepare_wide(v, n, base, ready):
                    v = v[:, :].rearrange("p (j f) -> p j f", f=VB)
                    nc.vector.tensor_tensor(v_sq[:, 0:n, :], v[:, :, 0:F], v[:, :, 0:F], ALU.mult).then_inc(wide_v_step, 1)
                    dve.wait_ge(wide_v_step, base + 1)
                    nc.vector.reduce_sum(v_sum[:, 0:n], v_sq[:, 0:n, :], AX_X).then_inc(wide_v_step, 1)
                    dve.wait_ge(wide_v_step, base + 2)
                    nc.vector.scalar_tensor_tensor(v[:, :, F], v_sum[:, 0:n], -0.5, v[:, :, F],
                                                   ALU.mult, ALU.add).then_inc(ready, 1)

                with dve.Fori(0, BODIES) as body:
                    for s in range(BODY_GROUPS):
                        dve.wait_ge(wide_v_landed[s], (body + 1) * 16)
                        prepare_wide(v_raw[s], GROUP, (body * BODY_GROUPS + s) * 2, wide_v_ready)
                prepare_wide(v_raw_tail, TAIL, GROUPS * 2, wide_v_tail_ready)
                dve.wait_ge(wide_chunk_summed, ALL_CHUNKS)
                for h in range(HALVES):
                    nc.vector.tensor_copy(half(terms, h)[F:VB, :], acc_hm[h][F:VB, :]).then_inc(wide_terms_step, 1)
                    nc.vector.tensor_copy(half(xv, h), acc_hm[h][0:F, :]).then_inc(wide_terms_step, 1)
                    dve.wait_ge(wide_terms_step, 2 * h + 2)
                    nc.vector.tensor_tensor(half(terms, h)[0:F, :], half(xv, h), half(xv, h),
                                            ALU.mult).then_inc(wide_squares_ready, 1)
                dve.wait_ge(y_stored, 16)
                dve.wait_ge(wide_y_summed, HALVES)
                nc.vector.tensor_scalar(y_sb[:, :], y_ps[:, 0:COLS], g_sb[:, :], None, ALU.add).then_inc(wide_y_ready, 1)

        @block.tensor
        def _(pe):
            def multiply(c, k, s, j0, first):
                pe.wait_ge(x_converted, c + 1)
                for j in range(CHUNK):
                    w = w_bf[s][:, j0 + j, :]
                    start = first and j == 0
                    for acc, cols in ((acc_hm, w[:, 0:P]), (acc_lc, w[:, P:WCOLS])):
                        for h in range(HALVES):
                            at = j * BATCH + h * BANK
                            mm = nc.tensor.matmul(acc[h][:, :], cols, x_bf[k][:, at:at + BANK], start=start, stop=False)
                mm.then_inc(chunk_summed, 1)

            def weigh(h, rows):
                for q in range(h * COLS // HALVES, (h + 1) * COLS // HALVES):
                    mm = nc.tensor.matmul(y_ps[:, q:q + 1], terms[0:rows, q * P:(q + 1) * P], term_weights[0:rows, :],
                                          start=True, stop=True)
                return mm

            def body_products(body, first):
                for k in range(BODY_CHUNKS):
                    s = k // PER_GROUP
                    if k % PER_GROUP == 0:
                        pe.wait_ge(w_ready, body * BODY_GROUPS + s + 1)
                    multiply(body * BODY_CHUNKS + k, k, s, k % PER_GROUP * CHUNK, first and k == 0)

            def multiply_tail(c):
                h, t, n, rows = TAIL_CHUNKS[c - CHUNKS]
                pe.wait_ge(x_converted, c + 1)
                for j in range(n):
                    w = w_bf_tail[0:rows, t + j, :]
                    x = x_bf[c % BODY_CHUNKS][0:rows, j * BANK:(j + 1) * BANK]
                    stop = t + j == TAIL - 1
                    nc.tensor.matmul(acc_hm[h][:, :], w[:, 0:P], x, start=False, stop=stop)
                    mm = nc.tensor.matmul(acc_lc[h][:, :], w[:, P:WCOLS], x, start=False, stop=stop)
                mm.then_inc(chunk_summed, 1)

            body_products(0, True)
            with pe.Fori(1, BODIES) as body:
                body_products(body, False)
            pe.wait_ge(w_tail_ready, 1)
            for c in range(CHUNKS, ALL_CHUNKS):
                multiply_tail(c)

            pe.wait_ge(constants_set, BODY_GROUPS + 5)
            for h in range(HALVES):
                pe.wait_ge(c_copied, h + 1)
                pe.wait_ge(squares_ready, h + 1)
                weigh(h, F + NPARTS).then_inc(y_summed, 1)
            pe.wait_ge(rows_flagged, 1)
            nc.tensor.matmul(count_ps[0:1, 0:1], row_wide[:, :], ones[:, :], start=True, stop=True).then_inc(wide_counted, 1)

            pe.wait_ge(flag_ready, 1)
            wide = pe.value_load(wide_count[0:1, 0:1], min_val=0, max_val=P)
            with pe.If(wide > 0):
                def multiply_wide(c, k, s, j0, first):
                    pe.wait_ge(wide_x_converted, c + 1)
                    for j in range(CHUNK):
                        w = v_raw[s][:, (j0 + j) * VB:(j0 + j + 1) * VB]
                        start = first and j == 0
                        for h in range(HALVES):
                            at = j * BATCH + h * BANK
                            mm = nc.tensor.matmul(acc_hm[h][0:VB, :], w, x_int[k][:, at:at + BANK].bitcast(F32),
                                                  start=start, stop=False)
                    mm.then_inc(wide_chunk_summed, 1)

                def wide_products(body, first):
                    for k in range(BODY_CHUNKS):
                        s = k // PER_GROUP
                        if k % PER_GROUP == 0:
                            pe.wait_ge(wide_v_ready, body * BODY_GROUPS + s + 1)
                        multiply_wide(body * BODY_CHUNKS + k, k, s, k % PER_GROUP * CHUNK, first and k == 0)

                wide_products(0, True)
                with pe.Fori(1, BODIES) as body:
                    wide_products(body, False)
                pe.wait_ge(wide_v_tail_ready, 1)
                for c in range(CHUNKS, ALL_CHUNKS):
                    h, t, n, rows = TAIL_CHUNKS[c - CHUNKS]
                    pe.wait_ge(wide_x_converted, c + 1)
                    for j in range(n):
                        mm = nc.tensor.matmul(acc_hm[h][0:VB, :], v_raw_tail[0:rows, (t + j) * VB:(t + j + 1) * VB],
                                              x_int[c % BODY_CHUNKS][0:rows, j * BANK:(j + 1) * BANK].bitcast(F32),
                                              start=False, stop=t + j == TAIL - 1)
                    mm.then_inc(wide_chunk_summed, 1)
                for h in range(HALVES):
                    pe.wait_ge(wide_squares_ready, h + 1)
                    weigh(h, VB).then_inc(wide_y_summed, 1)


def kernel(r_x, L0_rec_V, L0_rec_bias, L0_rec_g_bias):
    import numpy as _np
    import concourse.bacc as _bacc
    from concourse import mybir as _mybir
    from concourse.bass_utils import run_bass_kernel_spmd as _run

    rows = TILES * P
    x_t = _np.ascontiguousarray(_np.asarray(r_x).T)
    v_bias = _np.zeros((rows, VB), _np.float32)
    v_bias[:VOCAB, :F] = _np.asarray(L0_rec_V)
    v_bias[:VOCAB, F:] = _np.asarray(L0_rec_bias)
    v_main = v_bias[:TAIL_ROW].reshape(GROUPS, PER_GROUP, P, CHUNK, VB).transpose(0, 2, 1, 3, 4)
    v_tail = v_bias[TAIL_ROW:].reshape(TAIL, P, VB).transpose(1, 0, 2)
    arrays = {
        "x_t": x_t,
        "v_main": _np.ascontiguousarray(v_main).reshape(GROUPS, P, GROUP * VB),
        "v_tail": _np.ascontiguousarray(v_tail).reshape(P, TAIL * VB),
        "g_bias": _np.full((P, 1), _np.asarray(L0_rec_g_bias)),
    }

    nc = _bacc.Bacc("TRN2", target_bir_lowering=False, num_devices=1)
    args = [nc.dram_tensor(n, a.shape, _mybir.dt.from_np(a.dtype), kind="ExternalInput").ap() for n, a in arrays.items()]
    args.append(nc.dram_tensor("out", (P, COLS), _mybir.dt.float32, kind="ExternalOutput").ap())
    fm_kernel(nc, *args)
    r = _run(nc, [arrays], core_ids=[0])
    return _np.ascontiguousarray(r.results[0]["out"].T).reshape(BATCH, 1)
```
